# Optimizing a Trainium2 kernel written in Bass

```python
import numpy as np
import jax
import jax.numpy as jnp

def _softmax(x, axis=-1):
    return jax.nn.softmax(x, axis=axis)

def _gelu(x):
    return jax.nn.gelu(x, approximate=True)

def _silu(x):
    return jax.nn.silu(x)

def _sigmoid(x):
    return jax.nn.sigmoid(x)

def _layernorm(x, axis=-1, eps=1e-05):
    m = jnp.mean(x, axis=axis, keepdims=True)
    v = jnp.var(x, axis=axis, keepdims=True)
    return (x - m) / jnp.sqrt(v + eps)

def _scatter_add(tgt, idx, src, axis=0):
    return tgt.at[idx].add(src)

def _segment_sum(src, seg, n):
    return jax.ops.segment_sum(src, seg, n)
kernel_name = 'mk_adj_resnorm_d1_adj_r2_2039ce'

def setup_inputs(seed: int=0):
    np.random.seed(seed)
    _w = jnp.asarray

    def _rec_inputs():
        import jax
        import jax.numpy as jnp
        _gk = jax.random.key(seed)
        x = -0.003407 + 1.001 * jax.random.normal(jax.random.fold_in(_gk, 1), (1354, 128), jnp.float32)
        _a = jax.random.bernoulli(jax.random.fold_in(_gk, 2), 0.00590842, (1354, 1354))
        _a = jnp.logical_or(_a, jnp.swapaxes(_a, -1, -2))
        _a = jnp.logical_or(_a, jnp.eye(1354, dtype=bool))
        _af = _a.astype(jnp.float32)
        _af = _af * jax.random.uniform(jax.random.fold_in(_gk, 3), (1354, 1354), jnp.float32, 0.05, 1)
        adj = _af
        return (x, adj)
    x, adj = _rec_inputs()

    def _L0_gnn_setup():
        import jax, jax.numpy as jnp
        import numpy as np
        LN_EPS = 1e-05
        key = jax.random.key(seed)
        ks = jax.random.split(key, 6)
        N, D = (512, 128)
        return {'node_feats': jax.random.normal(ks[0], (N, D), dtype=jnp.float32), 'adj': jax.random.uniform(ks[1], (N, N), dtype=jnp.float32), 'msg_w': jax.random.normal(ks[2], (D, 2 * D), dtype=jnp.float32) * 0.05, 'msg_b': jax.random.normal(ks[3], (D,), dtype=jnp.float32) * 0.05, 'upd_w': jax.random.normal(ks[4], (D, 2 * D), dtype=jnp.float32) * 0.05, 'upd_b': jax.random.normal(ks[5], (D,), dtype=jnp.float32) * 0.05, 'ln_w': jnp.ones((D,), dtype=jnp.float32), 'ln_b': jnp.zeros((D,), dtype=jnp.float32)}
    _L0_gnn_all = _L0_gnn_setup()
    _L0_gnn_in = {k: v for k, v in _L0_gnn_all.items() if k in ('msg_w', 'msg_b', 'upd_w', 'upd_b', 'ln_w', 'ln_b')}
    del _L0_gnn_all
    return {'x': x, 'adj': adj, 'L0_gnn_msg_w': _L0_gnn_in['msg_w'], 'L0_gnn_msg_b': _L0_gnn_in['msg_b'], 'L0_gnn_upd_w': _L0_gnn_in['upd_w'], 'L0_gnn_upd_b': _L0_gnn_in['upd_b'], 'L0_gnn_ln_w': _L0_gnn_in['ln_w'], 'L0_gnn_ln_b': _L0_gnn_in['ln_b']}

def reference(x, adj, L0_gnn_msg_w, L0_gnn_msg_b, L0_gnn_upd_w, L0_gnn_upd_b, L0_gnn_ln_w, L0_gnn_ln_b):
    import jax
    import jax.numpy as jnp

    def _L0_gnn_ref(node_feats, adj, msg_w, msg_b, upd_w, upd_b, ln_w, ln_b):
        import jax, jax.numpy as jnp
        import numpy as np
        LN_EPS = 1e-05
        D = node_feats.shape[-1]
        s = node_feats @ msg_w[:, :D].T
        d = node_feats @ msg_w[:, D:].T
        messages = jax.nn.gelu(s[:, None, :] + d[None, :, :] + msg_b, approximate=False)
        aggregated = jnp.einsum('ijd,ij->id', messages, adj)
        combined = jnp.concatenate([node_feats, aggregated], axis=-1)
        new_feats = combined @ upd_w.T + upd_b
        h = jax.nn.gelu(new_feats, approximate=False) + node_feats
        mu = jnp.mean(h, axis=-1, keepdims=True)
        var = jnp.var(h, axis=-1, keepdims=True)
        return (h - mu) / jnp.sqrt(var + LN_EPS) * ln_w + ln_b
    x = _layernorm(x + _L0_gnn_ref(x, adj, L0_gnn_msg_w, L0_gnn_msg_b, L0_gnn_upd_w, L0_gnn_upd_b, L0_gnn_ln_w, L0_gnn_ln_b), axis=-1)
    return x

_drawn_inputs = setup_inputs


def setup_inputs(seed=0):
    import zlib

    import numpy as np

    out = dict(_drawn_inputs(seed))
    spreads = {'L0_gnn_ln_w': (1.0, 0.2), 'L0_gnn_ln_b': (0.0, 0.1)}
    factors = {'L0_gnn_upd_b': 3.354}
    for name, (base, spread) in spreads.items():
        noise = np.random.default_rng([zlib.crc32(name.encode()), seed]).standard_normal(out[name].shape)
        drawn = base * np.exp(spread * noise) if base else spread * noise
        out[name] = jnp.asarray(drawn.astype(out[name].dtype))
    for name, factor in factors.items():
        out[name] = (out[name] * factor).astype(out[name].dtype)
    return out
```

```python
import concourse.bass as bass
from concourse import mybir
from contextlib import ExitStack



def graph_layer(nc, x, adj, msg_w, msg_b, upd_w, upd_b, ln_w, ln_b, out):
    F32, I32, U32 = mybir.dt.float32, mybir.dt.int32, mybir.dt.uint32
    ALU, ACT, AX = mybir.AluOpType, mybir.ActivationFunctionType, mybir.AxisListType
    P = 128
    N, D = x.shape
    TILES = -(-N // P)
    LAST = N - (TILES - 1) * P
    PAIRS = (TILES - 1) // 2
    QUAD = 4
    QUADS = 7
    KEEP = QUAD * QUADS
    ROUNDS = KEEP // 8 + 1
    LISTED = 16
    EARLY = PAIRS - 1
    EPS = 1e-5
    CHUNKS = [(a, min(a + 512, N)) for a in range(0, N, 512)]
    GROUPS = [(a, min(a + 4, TILES)) for a in range(0, TILES, 4)]

    def rows(t):
        return LAST if t == TILES - 1 else P

    ctx = ExitStack()
    with ctx:
        def sb(name, shape, dt=F32):
            return ctx.enter_context(nc.sbuf_tensor(name, shape, dt))

        def sem(name):
            return ctx.enter_context(nc.semaphore(name))

        d_rows = nc.dram_tensor("d_rows", (N, D), F32, kind="Internal").ap()

        ident = sb("ident", [P, P])
        off_diag = sb("off_diag", [P, P])
        ones = sb("ones", [P, P])
        eps = sb("eps", [P, 1])
        row_no_i = sb("row_no_i", [P, TILES], I32)
        row_no = sb("row_no", [P, TILES])
        every_i = sb("every_i", [1, N], I32)
        every = sb("every", [1, N])

        x_sb = sb("x_sb", [P, TILES, D])
        xT = sb("xT", [P, TILES * P])
        w_in = sb("w_in", [P, 4, D])
        wT = sb("wT", [P, 4, D])
        msg_b_all = sb("msg_b_all", [P, D])
        msg_b_col = sb("msg_b_col", [P, 1])
        upd_b_row = sb("upd_b_row", [1, D])
        ln_w_all = sb("ln_w_all", [P, D])
        ln_b_all = sb("ln_b_all", [P, D])
        x_ln_b = sb("x_ln_b", [P, TILES, D])
        s_sb = sb("s_sb", [P, TILES, D])
        d_sb = sb("d_sb", [P, TILES, D])
        sT = sb("sT", [P, N])
        dT = sb("dT", [P, N])
        self_pre = sb("self_pre", [P, TILES, D])
        self_msg = sb("self_msg", [P, D])
        self_w = sb("self_w", [P, TILES])
        self_kept = sb("self_kept", [P, TILES])

        adj_sb = [sb(f"adj_sb{h}", [P, N]) for h in range(2)]
        left = sb("left", [P, N])
        top = sb("top", [P, 8 * ROUNDS])
        top_j = sb("top_j", [P, 8 * ROUNDS], U32)
        least = sb("least", [P, 1])
        more = sb("more", [P, 1])
        kept = sb("kept", [P, 1])
        full = sb("full", [P, TILES])
        weight = sb("weight", [P, TILES, KEEP])
        column = sb("column", [P, TILES, KEEP], U32)

        gather_j = [sb(f"gather_j{h}", [P, KEEP], U32) for h in range(2)]
        pre = [sb(f"pre{h}", [P, KEEP, D]) for h in range(2)]
        msg = sb("msg", [P, KEEP, D])
        diag = sb("diag", [P, KEEP, P])
        self_diag = sb("self_diag", [P, P])
        aggT = sb("aggT", [P, TILES * P])

        full_no = sb("full_no", [P, TILES])
        full_count = sb("full_count", [P, 1])
        count_sb = sb("count_sb", [P, 1])
        few = sb("few", [P, 1])
        many = sb("many", [P, 1])
        extra = sb("extra", [1, 1])
        full_line = sb("full_line", [1, P * TILES])
        picked = sb("picked", [1, LISTED])
        shift = sb("shift", [1, LISTED])
        rows_f = sb("rows_f", [1, N])
        rows_i = sb("rows_i", [1, N], I32)
        n_rows_f = sb("n_rows_f", [1, 1])
        n_rows_i = sb("n_rows_i", [1, 1], I32)
        adj_line = sb("adj_line", [P, N])
        line_msg = sb("line_msg", [P, N])
        line_out = sb("line_out", [P, N])
        line_sum = sb("line_sum", [P, 1])
        full_aggT = sb("full_aggT", [P, TILES * P])

        u_sb = sb("u_sb", [P, 2, D])
        h_sb = sb("h_sb", [P, 2, D])
        stats = sb("stats", [P, 2, 6])
        moments = sb("moments", [P, 2, 2])
        std = sb("std", [P, 2])
        rstd = sb("rstd", [P, 2])
        y_sb = sb("y_sb", [P, 2, D])
        out_sb = sb("out_sb", [P, TILES, D])

        bank = [ctx.enter_context(nc.psum_tensor(f"bank{b}", [P, 512], F32)) for b in range(8)]

        x_in = sem("x_in")
        w_loaded = sem("w_loaded")
        rows_loaded = sem("rows_loaded")
        consts = sem("consts")
        wT_raw = sem("wT_raw")
        wT_ready = sem("wT_ready")
        xT_raw = sem("xT_raw")
        xT_ready = sem("xT_ready")
        sd_raw = sem("sd_raw")
        s_ready = sem("s_ready")
        d_ready = sem("d_ready")
        d_stored = sem("d_stored")
        line_raw = sem("line_raw")
        line_ready = sem("line_ready")
        self_summed = sem("self_summed")
        adj_in = [sem(f"adj_in{h}") for h in range(2)]
        adj_used = sem("adj_used")
        search = sem("search")
        found = sem("found")
        pre_ready = sem("pre_ready")
        gathered = [[sem(f"gathered{h}_{q}") for q in range(QUADS)] for h in range(2)]
        self_weighted = sem("self_weighted")
        quad_ready = sem("quad_ready")
        summed = sem("summed")
        agg_ready = sem("agg_ready")
        step = sem("step")
        numbers_ready = sem("numbers_ready")
        line_in = sem("line_in")
        counts_ready = sem("counts_ready")
        counted = sem("counted")
        list_ready = sem("list_ready")
        adj_line_in = sem("adj_line_in")
        line_gelu = sem("line_gelu")
        line_step = sem("line_step")
        line_used = sem("line_used")
        merged = sem("merged")
        u_raw = sem("u_raw")
        u_ready = sem("u_ready")
        norm_step = sem("norm_step")
        var_ready = sem("var_ready")
        std_ready = sem("std_ready")
        gather_turn = sem("gather_turn")
        out_ready = sem("out_ready")
        stored = sem("stored")

        block = ctx.enter_context(nc.Block())

        LINES = len(CHUNKS)
        OUT_DMAS = PAIRS + 1

        def tile_cols(t, count=1):
            return bass.ds(t * P, count * P)

        @block.sync
        def _(sp):
            whole = (TILES - 1) * P
            sp.dma_start(x_sb[:, 0:TILES - 1, :],
                         x[0:whole, :].rearrange("(t p) d -> p t d", p=P)).then_inc(x_in, 16)
            sp.dma_start(x_sb[0:LAST, TILES - 1, :], x[whole:N, :]).then_inc(x_in, 16)
            for h in range(2):
                sp.dma_start(adj_sb[h][:, :], adj[h * P:(h + 1) * P, :]).then_inc(adj_in[h], 16)
            vec = lambda v: v.rearrange("(a d) -> a d", a=1)
            sp.dma_start(msg_b_all[:, :], vec(msg_b).to_broadcast([P, D])).then_inc(rows_loaded, 16)
            sp.dma_start(ln_w_all[:, :], vec(ln_w).to_broadcast([P, D])).then_inc(rows_loaded, 16)
            sp.dma_start(ln_b_all[:, :], vec(ln_b).to_broadcast([P, D])).then_inc(rows_loaded, 16)
            sp.dma_start(upd_b_row[:, :], vec(upd_b)).then_inc(rows_loaded, 16)
            sp.dma_start(msg_b_col[:, :], msg_b.rearrange("(d a) -> d a", a=1)).then_inc(rows_loaded, 16)
            line = adj.rearrange("i j -> (i j)")
            for t in range(TILES):
                n = rows(t)
                a = t * P * (N + 1)
                sp.dma_start(self_w[0:n, t:t + 1],
                             line[a:a + (n - 1) * (N + 1) + 1:N + 1].rearrange("(i a) -> i a", a=1),
                             allow_slow_non_contiguous=True).then_inc(rows_loaded, 16)

            with sp.Fori(1, PAIRS) as p:
                for h in range(2):
                    t = 2 * p + h
                    sp.wait_ge(adj_used, t - 1)
                    sp.dma_start(adj_sb[h][:, :], adj[bass.ds(t * P, P), :]).then_inc(adj_in[h], 16)
            sp.wait_ge(adj_used, TILES - 2)
            sp.dma_start(adj_sb[0][0:LAST, :], adj[whole:N, :]).then_inc(adj_in[0], 16)

            sp.wait_ge(numbers_ready, 1)
            sp.dma_start(full_line[0:1, :].rearrange("a (p t) -> a p t", t=TILES),
                         full_no[:, :]).then_inc(line_in, 16)

            sp.wait_ge(list_ready, 1)
            with sp.register("n_full_sp") as n_full, sp.register("row_sp") as row_reg:
                sp.reg_load(n_full, n_rows_i[0:1, 0:1])
                with sp.If_ne(n_full, 0):
                    with sp.Fori(0, sp.snap(n_full)) as r:
                        sp.reg_load(row_reg, rows_i[0:1, bass.ds(r, 1)])
                        row = sp.snap(row_reg)
                        sp.wait_ge(line_used, r + 1)
                        sp.dma_start(adj_line[:, :],
                                     adj[bass.ds(row, 1), :].to_broadcast([P, N])).then_inc(adj_line_in, 16)

            with sp.Fori(0, PAIRS) as p:
                sp.wait_ge(out_ready, 2 * p + 2)
                sp.dma_start(out[bass.ds(p * 2 * P, 2 * P), :].rearrange("(t p) d -> p t d", p=P),
                             out_sb[:, bass.ds(2 * p, 2), :]).then_inc(stored, 16)
            sp.wait_ge(out_ready, TILES)
            sp.dma_start(out[whole:N, :], out_sb[0:LAST, TILES - 1, :]).then_inc(stored, 16)
            sp.wait_ge(stored, 16 * OUT_DMAS)

        @block.gpsimd
        def _(pool):
            pool.memset(ident[:, :], 0.0).then_inc(consts, 1)
            pool.memset(ones[:, :], 1.0).then_inc(consts, 1)
            pool.wait_ge(consts, 2)
            pool.affine_select(out=ident[:, :], in_=ident[:, :], compare_op=ALU.not_equal, fill=1.0, base=0,
                               pattern=[[-1, P]], channel_multiplier=1).then_inc(consts, 1)
            pool.iota(row_no_i[:, :], pattern=[[P, TILES]], base=1, channel_multiplier=1).then_inc(consts, 1)
            pool.iota(every_i[:, :], pattern=[[1, N]], base=0, channel_multiplier=0).then_inc(consts, 1)
            pool.memset(full_aggT[:, :], 0.0).then_inc(consts, 1)
            pool.wait_ge(d_stored, 16 * (len(GROUPS) + 1))

            def gather(t, h, n):
                pool.wait_ge(pre_ready, 2 * t + 2)
                pool.sem_inc(gather_turn, 1)
                for q in range(QUADS):
                    for k in range(q * QUAD, (q + 1) * QUAD):
                        pool.indirect_dma_start(pre[h][0:n, k, :], None, d_rows[:, :],
                                                bass.IndirectOffsetOnAxis(ap=gather_j[h][0:n, k:k + 1], axis=0),
                                                compute_op=ALU.add).then_inc(gathered[h][q], 16)

            with pool.Fori(0, PAIRS) as p:
                for h in range(2):
                    gather(2 * p + h, h, P)
            gather(TILES - 1, 0, LAST)

        @block.scalar
        def _(act):
            vec2 = lambda w: w.rearrange("o (h k) -> o h k", h=2)
            act.dma_start(w_in[:, 0:2, :], vec2(msg_w)).then_inc(w_loaded, 16)
            act.dma_start(w_in[:, 2:4, :], vec2(upd_w)).then_inc(w_loaded, 16)
            act.wait_ge(wT_raw, 1)
            nc.scalar.copy(wT[:, :, :], bank[0][:, :].rearrange("p (a k) -> p a k", a=4)).then_inc(wT_ready, 1)
            whole = (TILES - 1) * P
            for g, (a, b) in enumerate(GROUPS):
                act.wait_ge(sd_raw, g + 1)
                full_tiles = b - a if b < TILES else b - a - 1
                src = bank[3 + 2 * (g % 2)]
                nc.scalar.copy(d_sb[:, a:a + full_tiles, :],
                               src[:, 0:full_tiles * D].rearrange("p (t d) -> p t d", d=D)).then_inc(d_ready, 1)
                if b == TILES:
                    nc.scalar.copy(d_sb[0:LAST, TILES - 1, :],
                                   src[0:LAST, full_tiles * D:(full_tiles + 1) * D]).then_inc(d_ready, 1)
                act.wait_ge(d_ready, g + 1)
                act.dma_start(d_rows[a * P:(a + full_tiles) * P, :].rearrange("(t p) d -> p t d", p=P),
                              d_sb[:, a:a + full_tiles, :]).then_inc(d_stored, 16)
            act.wait_ge(d_ready, len(GROUPS) + 1)
            act.dma_start(d_rows[whole:N, :], d_sb[0:LAST, TILES - 1, :]).then_inc(d_stored, 16)

            def prepare(t, h, n):
                act.wait_ge(found, t + 1)
                nc.scalar.copy(gather_j[h][0:n, :], column[0:n, bass.ds(t, 1), :]
                               .rearrange("p a k -> p (a k)")).then_inc(pre_ready, 1)
                nc.scalar.copy(pre[h][0:n, :, :],
                               s_sb[0:n, bass.ds(t, 1), :].to_broadcast([n, KEEP, D])).then_inc(pre_ready, 1)

            act.wait_ge(s_ready, len(GROUPS) + 1)
            prepare(0, 0, P)

            act.wait_ge(rows_loaded, 16 * (5 + TILES))
            for c, (a, b) in enumerate(CHUNKS):
                act.wait_ge(line_raw, 2 * c + 2)
                nc.scalar.activation(sT[:, a:b], bank[2 * c][:, 0:b - a], ACT.Identity,
                                     bias=msg_b_col[:, 0:1]).then_inc(line_ready, 1)
                nc.scalar.copy(dT[:, a:b], bank[2 * c + 1][:, 0:b - a]).then_inc(line_ready, 1)

            act.wait_ge(self_summed, 2)

            def weigh(t, h, n, more_tiles):
                if more_tiles:
                    prepare(t + 1, 1 - h, rows(TILES - 1) if more_tiles == "last" else P)
                nc.scalar.activation(self_msg[0:n, :], self_pre[0:n, bass.ds(t, 1), :].rearrange("p a d -> p (a d)"),
                                     ACT.Gelu).then_inc(self_weighted, 1)
                nc.scalar.activation(self_diag[0:n, 0:n], ident[0:n, 0:n], ACT.Copy,
                                     scale=self_kept[0:n, bass.ds(t, 1)]).then_inc(self_weighted, 1)
                for q in range(QUADS):
                    ks = slice(q * QUAD, (q + 1) * QUAD)
                    act.wait_ge(gathered[h][q], 16 * QUAD * (t // 2 + 1))
                    nc.scalar.activation(msg[0:n, ks, :], pre[h][0:n, ks, :], ACT.Gelu).then_inc(quad_ready, 1)
                    for k in range(q * QUAD, (q + 1) * QUAD):
                        nc.scalar.activation(diag[0:n, k, 0:n], ident[0:n, 0:n], ACT.Copy,
                                             scale=weight[0:n, bass.ds(t, 1), k]).then_inc(quad_ready, 1)
                act.wait_ge(summed, t + 1)
                nc.scalar.copy(aggT[:, bass.ds(t * P, n)], bank[6 + h][:, 0:n]).then_inc(agg_ready, 1)

            with act.Fori(0, EARLY) as p:
                for h in range(2):
                    weigh(2 * p + h, h, P, "whole")

            act.wait_ge(list_ready, 1)
            with act.register("n_full_act") as n_full, act.register("row_act") as row_reg:
                act.reg_load(n_full, n_rows_i[0:1, 0:1])
                with act.If_ne(n_full, 0):
                    with act.Fori(0, act.snap(n_full)) as r:
                        act.reg_load(row_reg, rows_i[0:1, bass.ds(r, 1)])
                        row = act.snap(row_reg)
                        act.wait_ge(line_used, r + 1)
                        nc.scalar.activation(line_msg[:, :], dT[:, :], ACT.Gelu,
                                             bias=sT[:, bass.ds(row, 1)]).then_inc(line_gelu, 1)

            def update(t, n, k):
                act.wait_ge(u_raw, t + k)
                nc.scalar.activation(u_sb[0:n, 0:k, :], bank[0][0:n, 0:k * D]
                                     .rearrange("p (t d) -> p t d", d=D), ACT.Gelu).then_inc(u_ready, k)
                for half in range(2):
                    act.wait_ge(var_ready, 2 * t + (half + 1) * k)
                    nc.scalar.activation(std[0:n, 0:k], moments[0:n, 0:k, 1], ACT.Sqrt,
                                         bias=eps[0:n, 0:1]).then_inc(std_ready, k)

            with act.Fori(0, EARLY) as p:
                update(2 * p, P, 2)
            weigh(2 * EARLY, 0, P, "whole")
            weigh(2 * EARLY + 1, 1, P, "last")
            update(2 * EARLY, P, 2)
            weigh(TILES - 1, 0, LAST, None)
            update(TILES - 1, LAST, 1)

        @block.vector
        def _(dve):
            dve.wait_ge(consts, 5)
            nc.vector.tensor_scalar(off_diag[:, :], ident[:, :], -1.0, 1.0, ALU.mult, ALU.add).then_inc(step, 1)
            nc.vector.tensor_copy(row_no[:, :], row_no_i[:, :]).then_inc(step, 1)
            nc.vector.tensor_copy(every[:, :], every_i[:, :]).then_inc(step, 1)
            nc.vector.memset(full[:, :], 0.0).then_inc(step, 1)
            nc.vector.memset(eps[:, :], EPS)
            for g, (a, b) in enumerate(GROUPS):
                n = min(b * P, N) - a * P
                dve.wait_ge(xT_raw, g + 1)
                nc.vector.tensor_copy(xT[:, a * P:a * P + n], bank[1 + g][:, 0:n]).then_inc(xT_ready, 1)
            dve.wait_ge(rows_loaded, 16 * (5 + TILES))
            for g, (a, b) in enumerate(GROUPS):
                dve.wait_ge(sd_raw, g + 1)
                full_tiles = b - a if b < TILES else b - a - 1
                src = bank[2 + 2 * (g % 2)]
                nc.vector.tensor_tensor(s_sb[:, a:a + full_tiles, :],
                                        src[:, 0:full_tiles * D].rearrange("p (t d) -> p t d", d=D),
                                        msg_b_all[:, :].unsqueeze(1).to_broadcast([P, full_tiles, D]),
                                        ALU.add).then_inc(s_ready, 1)
                if b == TILES:
                    nc.vector.tensor_tensor(s_sb[0:LAST, TILES - 1, :],
                                            src[0:LAST, full_tiles * D:(full_tiles + 1) * D],
                                            msg_b_all[0:LAST, :], ALU.add).then_inc(s_ready, 1)
            dve.wait_ge(s_ready, len(GROUPS) + 1)
            dve.wait_ge(d_ready, len(GROUPS) + 1)
            T1 = TILES - 1
            nc.vector.tensor_tensor(self_pre[:, 0:T1, :], s_sb[:, 0:T1, :], d_sb[:, 0:T1, :],
                                    ALU.add).then_inc(self_summed, 1)
            nc.vector.tensor_tensor(self_pre[0:LAST, T1, :], s_sb[0:LAST, T1, :], d_sb[0:LAST, T1, :],
                                    ALU.add).then_inc(self_summed, 1)
            dve.wait_ge(x_in, 32)
            nc.vector.tensor_tensor(x_ln_b[:, 0:T1, :], x_sb[:, 0:T1, :],
                                    ln_b_all[:, :].unsqueeze(1).to_broadcast([P, T1, D]), ALU.add)
            nc.vector.tensor_tensor(x_ln_b[0:LAST, T1, :], x_sb[0:LAST, T1, :], ln_b_all[0:LAST, :],
                                    ALU.add).then_inc(step, 1)
            dve.wait_ge(step, 5)

            def find(t, h, n):
                done = 0
                a, v, j = adj_sb[h], top, top_j
                dve.wait_ge(adj_in[h], 16 * (t // 2 + 1))
                nc.vector.tensor_tensor(a[0:n, bass.ds(t * P, n)], a[0:n, bass.ds(t * P, n)], off_diag[0:n, 0:n],
                                        ALU.mult).then_inc(search, 1)
                dve.wait_ge(search, 1)
                nc.vector.tensor_reduce(least[0:n, :], a[0:n, :], AX.X, ALU.min).then_inc(search, 1)
                done += 2
                for r in range(ROUNDS):
                    src = a if r == 0 else left
                    e = slice(8 * r, 8 * r + 8)
                    dve.wait_ge(search, done)
                    nc.vector.max(v[0:n, e], src[0:n, :]).then_inc(search, 1)
                    done += 1
                    dve.wait_ge(search, done)
                    nc.vector.max_index(j[0:n, e], v[0:n, e], src[0:n, :]).then_inc(search, 1)
                    done += 1
                    if r < ROUNDS - 1:
                        dve.wait_ge(search, done)
                        nc.vector.match_replace(left[0:n, :], v[0:n, e], src[0:n, :], 0.0).then_inc(search, 1)
                        done += 1
                    if r == 0:
                        dve.wait_ge(search, done)
                        dve.sem_inc(adj_used, 1)
                nc.vector.tensor_scalar(more[0:n, :], v[0:n, KEEP:KEEP + 1], 0.0, None,
                                        ALU.is_gt).then_inc(search, 1)
                done += 1
                dve.wait_ge(search, done)
                nc.vector.scalar_tensor_tensor(full[0:n, bass.ds(t, 1)], least[0:n, :], 0.0, more[0:n, :],
                                               ALU.is_lt, ALU.max).then_inc(search, 1)
                done += 1
                dve.wait_ge(search, done)
                nc.vector.tensor_scalar(kept[0:n, :], full[0:n, bass.ds(t, 1)], -1.0, 1.0,
                                        ALU.mult, ALU.add).then_inc(search, 1)
                done += 1
                nc.vector.tensor_copy(column[0:n, bass.ds(t, 1), :].rearrange("p a k -> p (a k)"),
                                      j[0:n, 0:KEEP]).then_inc(search, 1)
                done += 1
                dve.wait_ge(search, done)
                nc.vector.tensor_scalar(weight[0:n, bass.ds(t, 1), :].rearrange("p a k -> p (a k)"),
                                        v[0:n, 0:KEEP], kept[0:n, :], None, ALU.mult)
                nc.vector.tensor_tensor(self_kept[0:n, bass.ds(t, 1)], self_w[0:n, bass.ds(t, 1)],
                                        kept[0:n, :], ALU.mult).then_inc(found, 1)
                dve.sem_clear(search)

            with dve.Fori(0, PAIRS) as p:
                for h in range(2):
                    find(2 * p + h, h, P)
            find(TILES - 1, 0, LAST)
            dve.wait_ge(found, TILES)
            nc.vector.tensor_reduce(full_count[:, :], full[:, :], AX.X, ALU.add).then_inc(counts_ready, 1)
            nc.vector.tensor_tensor(full_no[:, :], full[:, :], row_no[:, :], ALU.mult).then_inc(numbers_ready, 1)
            dve.wait_ge(counted, 1)
            nc.vector.tensor_copy(count_sb[:, :], bank[2][:, 0:1]).then_inc(step, 1)
            dve.wait_ge(line_in, 16)
            nc.vector.max(picked[:, 0:8], full_line[:, :]).then_inc(step, 1)
            dve.wait_ge(step, 7)
            nc.vector.match_replace(full_line[:, :], picked[:, 0:8], full_line[:, :], 0.0).then_inc(step, 1)
            nc.vector.tensor_scalar(many[:, :], count_sb[:, :], float(LISTED), None, ALU.is_gt).then_inc(step, 1)
            dve.wait_ge(step, 9)
            nc.vector.max(picked[:, 8:16], full_line[:, :]).then_inc(step, 1)
            nc.vector.tensor_scalar(few[:, :], many[:, :], -1.0, 1.0, ALU.mult, ALU.add).then_inc(step, 1)
            nc.vector.tensor_scalar(extra[:, :], count_sb[0:1, :], -1.0, float(N), ALU.mult,
                                    ALU.add).then_inc(step, 1)
            dve.wait_ge(step, 12)
            nc.vector.scalar_tensor_tensor(n_rows_f[:, :], extra[:, :], many[0:1, :], count_sb[0:1, :],
                                           ALU.mult, ALU.add).then_inc(step, 1)
            nc.vector.tensor_scalar(picked[:, :], picked[:, :], -1.0, None, ALU.add).then_inc(step, 1)
            nc.vector.tensor_copy(rows_i[:, :], every[:, :]).then_inc(step, 1)
            dve.wait_ge(step, 15)
            nc.vector.tensor_copy(n_rows_i[:, :], n_rows_f[:, :])
            nc.vector.tensor_tensor(shift[:, :], every[:, 0:LISTED], picked[:, :], ALU.subtract).then_inc(step, 1)
            dve.wait_ge(step, 16)
            nc.vector.scalar_tensor_tensor(rows_f[:, 0:LISTED], shift[:, :], many[0:1, :], picked[:, :],
                                           ALU.mult, ALU.add).then_inc(step, 1)
            dve.wait_ge(step, 17)
            nc.vector.tensor_copy(rows_i[:, 0:LISTED], rows_f[:, 0:LISTED]).then_inc(list_ready, 1)

            dve.wait_ge(list_ready, 1)
            dve.wait_ge(consts, 6)
            with dve.register("n_full_dve") as n_full, dve.register("row_dve") as row_reg:
                dve.reg_load(n_full, n_rows_i[0:1, 0:1])
                with dve.If_ne(n_full, 0):
                    n_lines = dve.snap(n_full)
                    dve.sem_inc(line_used, 1)
                    with dve.Fori(0, n_lines) as r:
                        dve.reg_load(row_reg, rows_i[0:1, bass.ds(r, 1)])
                        row = dve.snap(row_reg)
                        dve.wait_ge(adj_line_in, 16 * (r + 1))
                        dve.wait_ge(line_gelu, r + 1)
                        nc.vector.tensor_tensor_reduce(out=line_out[:, :], in0=line_msg[:, :], in1=adj_line[:, :],
                                                       scale=1.0, scalar=0.0, op0=ALU.mult, op1=ALU.add,
                                                       accum_out=line_sum[:, 0:1]).then_inc(line_step, 1)
                        dve.wait_ge(line_step, 1)
                        nc.vector.tensor_copy(full_aggT[:, bass.ds(row, 1)], line_sum[:, 0:1]).then_inc(line_step, 1)
                        dve.wait_ge(line_step, 2)
                        dve.sem_clear(line_step)
                        dve.sem_inc(line_used, 1)

            def merge(t, cols):
                cs = slice(t * P, t * P + cols)
                nc.vector.scalar_tensor_tensor(aggT[:, cs], aggT[:, cs], few[:, 0:1], full_aggT[:, cs],
                                               ALU.mult, ALU.add).then_inc(merged, 1)

            def moments_of(src, t, n, k, half, at):
                for i in range(k):
                    nc.vector.bn_stats(stats[0:n, i, :], src[:, i, :]).then_inc(norm_step, 1)
                dve.wait_ge(norm_step, at + k)
                for i in range(k):
                    nc.vector.bn_aggr(moments[0:n, i, :], stats[0:n, i, :]).then_inc(var_ready, 1)
                dve.wait_ge(std_ready, 2 * t + (half + 1) * k)
                nc.vector.reciprocal(rstd[0:n, 0:k], std[0:n, 0:k]).then_inc(norm_step, k)
                dve.wait_ge(norm_step, at + 2 * k)

            def finish(t, n, k):
                at = 0
                ts = bass.ds(t, k)
                h, y = h_sb[0:n, 0:k, :], y_sb[0:n, 0:k, :]
                dve.wait_ge(u_ready, t + k)
                nc.vector.tensor_tensor(h, u_sb[0:n, 0:k, :], x_sb[0:n, ts, :], ALU.add).then_inc(norm_step, k)
                dve.wait_ge(norm_step, at + k)
                moments_of(h, t, n, k, 0, at + k)
                for i in range(k):
                    nc.vector.tensor_scalar(y[:, i, :], h[:, i, :], moments[0:n, i, 0:1], rstd[0:n, i:i + 1],
                                            ALU.subtract, ALU.mult).then_inc(norm_step, 1)
                dve.wait_ge(norm_step, at + 4 * k)
                nc.vector.tensor_tensor(h, y, ln_w_all[0:n, :].unsqueeze(1).to_broadcast([n, k, D]),
                                        ALU.mult).then_inc(norm_step, k)
                dve.wait_ge(norm_step, at + 5 * k)
                nc.vector.tensor_tensor(y, h, x_ln_b[0:n, ts, :], ALU.add).then_inc(norm_step, k)
                dve.wait_ge(norm_step, at + 6 * k)
                moments_of(y, t, n, k, 1, at + 6 * k)
                for i in range(k):
                    nc.vector.tensor_scalar(out_sb[0:n, bass.ds(t + i, 1), :].rearrange("p a d -> p (a d)"),
                                            y[:, i, :], moments[0:n, i, 0:1], rstd[0:n, i:i + 1],
                                            ALU.subtract, ALU.mult).then_inc(out_ready, 1)
                dve.sem_clear(norm_step)

            dve.wait_ge(agg_ready, 2 * EARLY)
            merge(0, 2 * EARLY * P)
            with dve.Fori(0, EARLY) as p:
                finish(2 * p, P, 2)
            dve.wait_ge(agg_ready, 2 * EARLY + 2)
            merge(2 * EARLY, 2 * P)
            finish(2 * EARLY, P, 2)
            dve.wait_ge(agg_ready, TILES)
            merge(TILES - 1, LAST)
            finish(TILES - 1, LAST, 1)

        @block.tensor
        def _(pe):
            pe.wait_ge(consts, 5)
            pe.wait_ge(w_loaded, 32)
            for i in range(4):
                last = nc.tensor.transpose(bank[0][:, i * P:(i + 1) * P], w_in[:, i, :], ident[:, :])
            last.then_inc(wT_raw, 1)
            pe.wait_ge(x_in, 32)
            for g, (a, b) in enumerate(GROUPS):
                for t in range(a, b):
                    n = rows(t)
                    last = nc.tensor.transpose(bank[1 + g][:, (t - a) * P:(t - a) * P + n], x_sb[0:n, t, :],
                                               ident[0:n, 0:n])
                last.then_inc(xT_raw, 1)
            pe.wait_ge(wT_ready, 1)
            pe.wait_ge(xT_ready, len(GROUPS))
            for g, (a, b) in enumerate(GROUPS):
                if g >= 2:
                    pe.wait_ge(s_ready, g - 1)
                    pe.wait_ge(d_ready, g - 1)
                for side in range(2):
                    for t in range(a, b):
                        n = rows(t)
                        last = nc.tensor.matmul(bank[2 + 2 * (g % 2) + side][0:n, (t - a) * D:(t - a + 1) * D],
                                                xT[:, t * P:t * P + n], wT[:, side, :], start=True, stop=True)
                last.then_inc(sd_raw, 1)
            pe.wait_ge(s_ready, len(GROUPS) + 1)
            pe.wait_ge(d_ready, len(GROUPS) + 1)
            for c, (a, b) in enumerate(CHUNKS):
                for side in range(2):
                    nc.tensor.matmul(bank[2 * c + side][:, 0:b - a], wT[:, side, :], xT[:, a:b],
                                     start=True, stop=True).then_inc(line_raw, 1)

            def add_up(t, h, n):
                pe.wait_ge(self_weighted, 2 * t + 2)
                nc.tensor.matmul(bank[6 + h][:, 0:n], self_msg[0:n, :], self_diag[0:n, 0:n], start=True, stop=False)
                for q in range(QUADS):
                    pe.wait_ge(quad_ready, (QUAD + 1) * (t * QUADS + q + 1))
                    for k in range(q * QUAD, (q + 1) * QUAD):
                        last = nc.tensor.matmul(bank[6 + h][:, 0:n], msg[0:n, k, :], diag[0:n, k, 0:n],
                                                start=False, stop=(k == KEEP - 1))
                last.then_inc(summed, 1)

            def project(t, h, n):
                o = bank[0][0:n, h * D:(h + 1) * D]
                nc.tensor.matmul(o, xT[:, bass.ds(t * P, n)], wT[:, 2, :], start=True, stop=False)
                nc.tensor.matmul(o, aggT[:, bass.ds(t * P, n)], wT[:, 3, :], start=False, stop=False)
                nc.tensor.matmul(o, ones[0:1, 0:n], upd_b_row[0:1, :], start=False, stop=True).then_inc(u_raw, 1)

            pe.wait_ge(line_ready, 2 * LINES)
            with pe.Fori(0, EARLY) as p:
                for h in range(2):
                    add_up(2 * p + h, h, P)
            pe.wait_ge(counts_ready, 1)
            nc.tensor.matmul(bank[2][:, 0:1], ones[:, :], full_count[:, :], start=True, stop=True).then_inc(counted, 1)
            pe.wait_ge(rows_loaded, 16 * (5 + TILES))
            pe.wait_ge(merged, 1)
            for p in range(EARLY):
                if p:
                    pe.wait_ge(u_ready, 2 * p)
                for h in range(2):
                    project(2 * p + h, h, P)
            t = 2 * EARLY
            add_up(t, 0, P)
            add_up(t + 1, 1, P)
            pe.wait_ge(u_ready, t)
            pe.wait_ge(merged, 2)
            project(t, 0, P)
            project(t + 1, 1, P)
            add_up(TILES - 1, 0, LAST)
            pe.wait_ge(u_ready, TILES - 1)
            pe.wait_ge(merged, 3)
            project(TILES - 1, 0, LAST)


_INS = ["x", "adj", "L0_gnn_msg_w", "L0_gnn_msg_b", "L0_gnn_upd_w", "L0_gnn_upd_b", "L0_gnn_ln_w", "L0_gnn_ln_b"]


def kernel(**inputs):
    import numpy as _np
    import concourse.bacc as _bacc
    from concourse.bass_utils import run_bass_kernel_spmd as _run

    nc = _bacc.Bacc("TRN2", target_bir_lowering=False, num_devices=1)
    arrays, args = {}, []
    for name in _INS:
        a = _np.ascontiguousarray(inputs[name])
        arrays[f"in_{name}"] = a
        args.append(nc.dram_tensor(f"in_{name}", a.shape, mybir.dt.from_np(a.dtype), kind="ExternalInput").ap())
    shape = inputs["x"].shape
    args.append(nc.dram_tensor("out_0", shape, mybir.dt.float32, kind="ExternalOutput").ap())
    graph_layer(nc, *args)
    r = _run(nc, [arrays], core_ids=[0])
    return r.results[0]["out_0"]
```
